# Optimizing a Trainium2 kernel written in Bass

```python
import numpy as np
import jax
import jax.numpy as jnp

def _softmax(x, axis=-1):
    return jax.nn.softmax(x, axis=axis)

def _gelu(x):
    return jax.nn.gelu(x, approximate=True)

def _silu(x):
    return jax.nn.silu(x)

def _sigmoid(x):
    return jax.nn.sigmoid(x)

def _layernorm(x, axis=-1, eps=1e-05):
    m = jnp.mean(x, axis=axis, keepdims=True)
    v = jnp.var(x, axis=axis, keepdims=True)
    return (x - m) / jnp.sqrt(v + eps)

def _scatter_add(tgt, idx, src, axis=0):
    return tgt.at[idx].add(src)

def _segment_sum(src, seg, n):
    return jax.ops.segment_sum(src, seg, n)
kernel_name = 'mk_adj_ffn_d2_adj_r2_ffb9df'

def setup_inputs(seed: int=0):
    np.random.seed(seed)
    _w = jnp.asarray

    def _rec_inputs():
        import jax
        import jax.numpy as jnp
        _gk = jax.random.key(seed)
        x = -0.0005207 + 1.001 * jax.random.normal(jax.random.fold_in(_gk, 1), (2048, 128), jnp.float32)
        _w = (1.0 + jnp.arange(2048, dtype=jnp.float32)) ** (-0.5)
        _w = _w / _w.mean()
        _pij = jnp.clip(0.00390625 * _w[:, None] * _w[None, :], 0.0, 1.0)
        _a = jax.random.uniform(jax.random.fold_in(_gk, 2), (2048, 2048)) < _pij
        _a = jnp.logical_or(_a, jnp.eye(2048, dtype=bool))
        _af = _a.astype(jnp.float32)
        adj = _af
        return (x, adj)
    x, adj = _rec_inputs()

    def _L0_gnn_setup():
        import jax, jax.numpy as jnp
        import numpy as np
        N = 4096
        D_IN = 128
        D_OUT = 128
        key = jax.random.key(seed)
        k_x, k_a, k_w, k_bias = jax.random.split(key, 4)
        x = jax.random.normal(k_x, (N, D_IN), dtype=jnp.float32)
        A_shape = jax.random.randint(k_a, (N, N), 0, 2).astype(jnp.float32)
        A_shape = A_shape.at[jnp.arange(N), jnp.arange(N)].set(1.0)
        lim = 1.0 / np.sqrt(D_IN)
        W = jax.random.uniform(k_w, (D_OUT, D_IN), jnp.float32, -lim, lim)
        bias = jax.random.uniform(k_bias, (D_OUT,), jnp.float32, -lim, lim)
        b = jnp.ones((1,), dtype=jnp.float32)
        return {'x': x, 'A_shape': A_shape, 'W': W, 'bias': bias, 'b': b}
    _L0_gnn_all = _L0_gnn_setup()
    _L0_gnn_in = {k: v for k, v in _L0_gnn_all.items() if k in ('W', 'bias', 'b')}
    del _L0_gnn_all

    def _L0_ffn_setup():
        import jax, jax.numpy as jnp
        import numpy as np
        D_MODEL = 128
        N_EXPERTS = 16
        HIDDEN = 256
        SCALE = 0.02
        key = jax.random.key(seed)
        ks = jax.random.split(key, 5)
        x = jax.random.normal(ks[0], (4, 4096, D_MODEL), dtype=jnp.float32)
        gate_w = jax.random.normal(ks[1], (D_MODEL, N_EXPERTS), dtype=jnp.float32) * SCALE
        gate_b = jnp.zeros((N_EXPERTS,), dtype=jnp.float32)
        w1 = jax.random.normal(ks[2], (N_EXPERTS, D_MODEL, HIDDEN), dtype=jnp.float32) * SCALE
        w2 = jax.random.normal(ks[3], (N_EXPERTS, D_MODEL, HIDDEN), dtype=jnp.float32) * SCALE
        w3 = jax.random.normal(ks[4], (N_EXPERTS, HIDDEN, D_MODEL), dtype=jnp.float32) * SCALE
        return {'x': x, 'gate_w': gate_w, 'gate_b': gate_b, 'w1': w1, 'w2': w2, 'w3': w3}
    _L0_ffn_all = _L0_ffn_setup()
    _L0_ffn_in = {k: v for k, v in _L0_ffn_all.items() if k in ('gate_w', 'gate_b', 'w1', 'w2', 'w3')}
    del _L0_ffn_all

    def _L1_gnn_setup():
        import jax, jax.numpy as jnp
        import numpy as np
        D_IN = 128
        D_ATTN = 64
        STEPS = 2
        TOP_P = 0.9
        TAU = 1.0
        LN_EPS = 1e-05
        N_NODES = 4096

        def _top_p_attention(X, W1, W2, W3):
            q = X @ W1.T @ W2.T
            k = X @ W3.T
            logits = q @ k.T / TAU
            probs = jax.nn.softmax(logits, axis=-1)
            idx = jnp.argsort(-probs, axis=-1)
            sp = jnp.take_along_axis(probs, idx, axis=-1)
            cs = jnp.cumsum(sp, axis=-1)
            keep_sorted = cs - sp < TOP_P
            rows = jnp.arange(probs.shape[0])[:, None]
            mask = jnp.zeros(probs.shape, dtype=bool).at[rows, idx].set(keep_sorted)
            A = probs * mask
            return A / jnp.maximum(A.sum(-1, keepdims=True), 1e-12)
        key = jax.random.key(seed)
        ks = jax.random.split(key, 8)
        N, d, da, steps = (N_NODES, D_IN, D_ATTN, STEPS)
        X = jax.random.normal(ks[0], (N, d), dtype=jnp.float32)
        S = jax.random.uniform(ks[1], (N, N), dtype=jnp.float32)
        W1 = jax.random.normal(ks[2], (da, d), dtype=jnp.float32) / np.sqrt(d)
        W2 = jax.random.normal(ks[3], (da, da), dtype=jnp.float32) / np.sqrt(da)
        W3 = jax.random.normal(ks[4], (da, d), dtype=jnp.float32) / np.sqrt(d)
        U1 = jax.random.normal(ks[5], (steps, d, d), dtype=jnp.float32) / np.sqrt(d)
        U2 = jax.random.normal(ks[6], (steps, d, d), dtype=jnp.float32) / np.sqrt(d)
        ln_g = jnp.ones((d,), dtype=jnp.float32)
        ln_b = jnp.zeros((d,), dtype=jnp.float32)
        return {'X': X, 'S': S, 'W1': W1, 'W2': W2, 'W3': W3, 'U1': U1, 'U2': U2, 'ln_g': ln_g, 'ln_b': ln_b}
    _L1_gnn_all = _L1_gnn_setup()
    _L1_gnn_in = {k: v for k, v in _L1_gnn_all.items() if k in ('W1', 'W2', 'W3', 'U1', 'U2', 'ln_g', 'ln_b')}
    del _L1_gnn_all

    def _L1_ffn_setup():
        import math
        import jax, jax.numpy as jnp
        import numpy as np
        CAPACITY_FACTOR = 1.25
        TOP_K = 2
        LN_EPS = 1e-05

        def _layer_norm(x, gamma, beta):
            mu = jnp.mean(x, axis=-1, keepdims=True)
            var = jnp.var(x, axis=-1, keepdims=True)
            return (x - mu) * jax.lax.rsqrt(var + LN_EPS) * gamma + beta
        key = jax.random.key(seed)
        ks = jax.random.split(key, 4)
        B, S, D, F, E = (8, 2048, 128, 256, 8)
        x = jax.random.normal(ks[0], (B, S, D), dtype=jnp.float32)
        Wr = jax.random.normal(ks[1], (D, E), dtype=jnp.float32) / np.sqrt(D)
        br = jnp.zeros((E,), jnp.float32)
        W1 = jax.random.normal(ks[2], (E, D, F), dtype=jnp.float32) / np.sqrt(D)
        b1 = jnp.zeros((E, F), jnp.float32)
        W2 = jax.random.normal(ks[3], (E, F, D), dtype=jnp.float32) / np.sqrt(F)
        b2 = jnp.zeros((E, D), jnp.float32)
        gamma = jnp.ones((D,), jnp.float32)
        beta = jnp.zeros((D,), jnp.float32)
        return {'x': x, 'Wr': Wr, 'br': br, 'W1': W1, 'b1': b1, 'W2': W2, 'b2': b2, 'gamma': gamma, 'beta': beta}
    _L1_ffn_all = _L1_ffn_setup()
    _L1_ffn_in = {k: v for k, v in _L1_ffn_all.items() if k in ('Wr', 'br', 'W1', 'b1', 'W2', 'b2', 'gamma', 'beta')}
    del _L1_ffn_all
    return {'x': x, 'adj': adj, 'L0_gnn_W': _L0_gnn_in['W'], 'L0_gnn_bias': _L0_gnn_in['bias'], 'L0_gnn_b': _L0_gnn_in['b'], 'L0_ffn_gate_w': _L0_ffn_in['gate_w'], 'L0_ffn_gate_b': _L0_ffn_in['gate_b'], 'L0_ffn_w1': _L0_ffn_in['w1'], 'L0_ffn_w2': _L0_ffn_in['w2'], 'L0_ffn_w3': _L0_ffn_in['w3'], 'L1_gnn_W1': _L1_gnn_in['W1'], 'L1_gnn_W2': _L1_gnn_in['W2'], 'L1_gnn_W3': _L1_gnn_in['W3'], 'L1_gnn_U1': _L1_gnn_in['U1'], 'L1_gnn_U2': _L1_gnn_in['U2'], 'L1_gnn_ln_g': _L1_gnn_in['ln_g'], 'L1_gnn_ln_b': _L1_gnn_in['ln_b'], 'L1_ffn_Wr': _L1_ffn_in['Wr'], 'L1_ffn_br': _L1_ffn_in['br'], 'L1_ffn_W1': _L1_ffn_in['W1'], 'L1_ffn_b1': _L1_ffn_in['b1'], 'L1_ffn_W2': _L1_ffn_in['W2'], 'L1_ffn_b2': _L1_ffn_in['b2'], 'L1_ffn_gamma': _L1_ffn_in['gamma'], 'L1_ffn_beta': _L1_ffn_in['beta']}

def reference(x, adj, L0_gnn_W, L0_gnn_bias, L0_gnn_b, L0_ffn_gate_w, L0_ffn_gate_b, L0_ffn_w1, L0_ffn_w2, L0_ffn_w3, L1_gnn_W1, L1_gnn_W2, L1_gnn_W3, L1_gnn_U1, L1_gnn_U2, L1_gnn_ln_g, L1_gnn_ln_b, L1_ffn_Wr, L1_ffn_br, L1_ffn_W1, L1_ffn_b1, L1_ffn_W2, L1_ffn_b2, L1_ffn_gamma, L1_ffn_beta):
    import jax
    import jax.numpy as jnp

    def _L0_gnn_ref(x, A_shape, W, bias, b):
        import jax, jax.numpy as jnp
        import numpy as np
        N = 4096
        D_IN = 128
        D_OUT = 128
        y = jnp.linalg.norm(x, axis=-1, keepdims=True)
        A = x @ x.T / (y @ y.T)
        A = A * b
        A = jnp.tanh(A / 8.0) * 8.0
        A = jnp.exp(A) * A_shape
        A = A / jnp.sum(A, axis=-1, keepdims=True)
        x = A @ x
        return x @ W.T + bias

    def _L0_ffn_ref(x, gate_w, gate_b, w1, w2, w3):
        import jax, jax.numpy as jnp
        import numpy as np
        D_MODEL = 128
        N_EXPERTS = 16
        HIDDEN = 256
        SCALE = 0.02
        n_experts = w1.shape[0]
        logits = jnp.einsum('bsd,de->bse', x, gate_w) + gate_b
        probs = jax.nn.softmax(logits, axis=-1)
        top_probs, top_idx = jax.lax.top_k(probs, 2)
        top_probs = top_probs / jnp.sum(top_probs, axis=-1, keepdims=True)
        dispatch = jnp.sum(jax.nn.one_hot(top_idx, n_experts, dtype=x.dtype) * top_probs[..., None], axis=-2)
        h1 = jnp.einsum('bsd,edh->bseh', x, w1)
        h2 = jnp.einsum('bsd,edh->bseh', x, w2)
        hidden = jax.nn.silu(h1) * h2
        expert_out = jnp.einsum('bseh,eho->bseo', hidden, w3)
        return jnp.einsum('bseo,bse->bso', expert_out, dispatch)

    def _L1_gnn_ref(X, S, W1, W2, W3, U1, U2, ln_g, ln_b):
        import jax, jax.numpy as jnp
        import numpy as np
        D_IN = 128
        D_ATTN = 64
        STEPS = 2
        TOP_P = 0.9
        TAU = 1.0
        LN_EPS = 1e-05
        N_NODES = 4096

        def _top_p_attention(X, W1, W2, W3):
            q = X @ W1.T @ W2.T
            k = X @ W3.T
            logits = q @ k.T / TAU
            probs = jax.nn.softmax(logits, axis=-1)
            idx = jnp.argsort(-probs, axis=-1)
            sp = jnp.take_along_axis(probs, idx, axis=-1)
            cs = jnp.cumsum(sp, axis=-1)
            keep_sorted = cs - sp < TOP_P
            rows = jnp.arange(probs.shape[0])[:, None]
            mask = jnp.zeros(probs.shape, dtype=bool).at[rows, idx].set(keep_sorted)
            A = probs * mask
            return A / jnp.maximum(A.sum(-1, keepdims=True), 1e-12)
        N = X.shape[0]
        R = S + jnp.eye(N, dtype=X.dtype)
        R = R / R.sum(-1, keepdims=True)
        Z = jnp.zeros_like(X)
        Xf = X
        Xa = X
        for n in range(STEPS):
            A = _top_p_attention(Xa, W1, W2, W3)
            Xf = R @ Xf
            Xa = A @ Xa
            Z = Z + Xf @ U1[n].T + Xa @ U2[n].T
        h = X + Z
        mu = h.mean(-1, keepdims=True)
        var = jnp.mean((h - mu) ** 2, axis=-1, keepdims=True)
        return (h - mu) / jnp.sqrt(var + LN_EPS) * ln_g + ln_b

    def _L1_ffn_ref(x, Wr, br, W1, b1, W2, b2, gamma, beta):
        import math
        import jax, jax.numpy as jnp
        import numpy as np
        CAPACITY_FACTOR = 1.25
        TOP_K = 2
        LN_EPS = 1e-05

        def _layer_norm(x, gamma, beta):
            mu = jnp.mean(x, axis=-1, keepdims=True)
            var = jnp.var(x, axis=-1, keepdims=True)
            return (x - mu) * jax.lax.rsqrt(var + LN_EPS) * gamma + beta
        B, S, D = x.shape
        E = Wr.shape[1]
        N = B * S
        K = TOP_K
        logits = jnp.mean(x, axis=1) @ Wr + br
        routing_weights = jax.nn.softmax(logits, axis=-1)
        capacity = float(math.ceil(N * CAPACITY_FACTOR / E))
        expected_loads = routing_weights.sum(axis=0) * (N / B)
        scale = jnp.where(expected_loads > capacity, capacity / expected_loads, 1.0)
        routing_weights = jax.nn.softmax(routing_weights * scale, axis=-1)
        rw_tok = jnp.broadcast_to(routing_weights[:, None, :], (B, S, E)).reshape(N, E)
        top_w, top_i = jax.lax.top_k(rw_tok, K)
        top_w = jax.nn.softmax(top_w, axis=-1)
        xf = x.reshape(N, D)
        h = jax.nn.gelu(jnp.einsum('nd,edf->enf', xf, W1) + b1[:, None, :], approximate=False)
        y = jnp.einsum('enf,efd->end', h, W2) + b2[:, None, :]
        w_dense = jnp.zeros((N, E), x.dtype).at[jnp.arange(N)[:, None], top_i].add(top_w)
        out = jnp.einsum('ne,end->nd', w_dense, y).reshape(B, S, D)
        out = _layer_norm(out + x, gamma, beta)
        return out
    x = x + _L0_gnn_ref(_layernorm(x, axis=-1), adj, L0_gnn_W, L0_gnn_bias, L0_gnn_b)
    x = x + _L0_ffn_ref(_layernorm(x, axis=-1)[None], L0_ffn_gate_w, L0_ffn_gate_b, L0_ffn_w1, L0_ffn_w2, L0_ffn_w3)[0]
    x = x + _L1_gnn_ref(_layernorm(x, axis=-1), adj, L1_gnn_W1, L1_gnn_W2, L1_gnn_W3, L1_gnn_U1, L1_gnn_U2, L1_gnn_ln_g, L1_gnn_ln_b)
    x = x + _L1_ffn_ref(_layernorm(x, axis=-1)[None], L1_ffn_Wr, L1_ffn_br, L1_ffn_W1, L1_ffn_b1, L1_ffn_W2, L1_ffn_b2, L1_ffn_gamma, L1_ffn_beta)[0]
    return x

_drawn_inputs = setup_inputs


def setup_inputs(seed=0):
    import zlib

    import numpy as np

    out = dict(_drawn_inputs(seed))
    spreads = {'L0_ffn_gate_b': (0.0, 2.0),
     'L1_gnn_ln_g': (1.0, 0.2),
     'L1_gnn_ln_b': (0.0, 0.1),
     'L1_ffn_br': (0.0, 0.1),
     'L1_ffn_b1': (0.0, 0.516),
     'L1_ffn_b2': (0.0, 0.351),
     'L1_ffn_gamma': (1.0, 0.2),
     'L1_ffn_beta': (0.0, 0.1)}
    factors = {'L0_ffn_gate_w': 13.52}
    for name, (base, spread) in spreads.items():
        noise = np.random.default_rng([zlib.crc32(name.encode()), seed]).standard_normal(out[name].shape)
        drawn = base * np.exp(spread * noise) if base else spread * noise
        out[name] = jnp.asarray(drawn.astype(out[name].dtype))
    for name, factor in factors.items():
        out[name] = (out[name] * factor).astype(out[name].dtype)
    return out
```

```python
import math
from contextlib import ExitStack

import concourse.bass as bass
from concourse import mybir

ALU = mybir.AluOpType
ACT = mybir.ActivationFunctionType
F32 = mybir.dt.float32
BF16 = mybir.dt.bfloat16
I32 = mybir.dt.int32
U32 = mybir.dt.uint32
AX_X = mybir.AxisListType.X

P = 128
N = 2048
D = 128
NT = N // P
CH = 512
NC = N // CH
TPC = CH // P
LN_EPS = 1e-5


class Chain:

    def __init__(self, eng, sem):
        self.eng, self.sem, self.base, self.n = eng, sem, 0, 0

    def mark(self, ins):
        ins.then_inc(self.sem, 1)
        self.n += 1

    def sync(self):
        self.eng.wait_ge(self.sem, self.base + self.n)

    def link(self, ins):
        self.mark(ins)
        self.sync()

    def enter(self, i, per):
        self.outer, self.per = self.n, per
        self.base = i * per + self.outer
        self.n = 0

    def leave(self, times):
        assert self.n == self.per, f"the loop's body marks {self.n}"
        self.base, self.n = 0, self.outer + times * self.per


def bcast(ap, shape):
    return ap.to_broadcast(shape)


def build(nc, x, adj, L0_gnn_W, L0_gnn_bias, L0_gnn_b, L0_ffn_gate_w, L0_ffn_gate_b, L0_ffn_w1,
          L0_ffn_w2, L0_ffn_w3, L1_gnn_W1, L1_gnn_W2, L1_gnn_W3, L1_gnn_U1, L1_gnn_U2, L1_gnn_ln_g,
          L1_gnn_ln_b, L1_ffn_Wr, L1_ffn_br, L1_ffn_W1, L1_ffn_b1, L1_ffn_W2, L1_ffn_b2,
          L1_ffn_gamma, L1_ffn_beta, out, stop_after="D"):
    with ExitStack() as ctx:
        def sb(name, shape, dt=F32):
            return ctx.enter_context(nc.sbuf_tensor(name, shape, dt))

        def sem(name):
            return ctx.enter_context(nc.semaphore(name))

        adjT = sb("adjT", [P, NT, N], BF16)
        big = sb("big", [P, 16384])
        res = sb("res", [P, NT, D])
        xn = sb("xn", [P, NT, D])
        xnT = sb("xnT", [P, N])
        stats = sb("stats", [P, NT, 6])
        mean = sb("mean", [P, NT])
        var = sb("var", [P, NT])
        tmp16 = sb("tmp16", [P, NT])
        powin = sb("powin", [P, 2, NT])
        powout = sb("powout", [P, 2, NT])
        minus_half = sb("minus_half", [P, 2, NT])
        ident = sb("ident", [P, P])
        identb = sb("identb", [P, P], BF16)
        ones = sb("ones", [P, P])
        rowsum = sb("rowsum", [P, NT])
        bank = ctx.enter_context(nc.psum_tensor("bank", [P, 8, CH], F32))
        bankb = bank[:, :, :].bitcast(BF16)

        pow_asked = sem("pow_asked")
        pow_done = sem("pow_done")
        pows = [0]
        resflat = res[:, :, :].rearrange("p t d -> p (t d)")

        def carve(*sizes):
            at, views = 0, []
            for s in sizes:
                views.append(big[:, at:at + s])
                at += s
            assert at <= 16384
            return views

        def moments(dve, ch, src):
            for t in range(NT):
                ch.mark(nc.vector.bn_stats(stats[:, t, :], src[:, t, :]))
            ch.sync()
            ch.mark(nc.vector.tensor_tensor(mean[:, :], stats[:, :, 1], stats[:, :, 4], ALU.add))
            ch.mark(nc.vector.tensor_tensor(tmp16[:, :], stats[:, :, 1], stats[:, :, 4], ALU.subtract))
            ch.link(nc.vector.tensor_tensor(var[:, :], stats[:, :, 2], stats[:, :, 5], ALU.add))
            ch.mark(nc.vector.tensor_scalar(mean[:, :], mean[:, :], 0.5, None, ALU.mult))
            ch.mark(nc.vector.tensor_tensor(tmp16[:, :], tmp16[:, :], tmp16[:, :], ALU.mult))
            ch.link(nc.vector.tensor_scalar(var[:, :], var[:, :], 1.0 / D, None, ALU.mult))
            ch.link(nc.vector.scalar_tensor_tensor(out=var[:, :], in0=tmp16[:, :], scalar=0.25, in1=var[:, :],
                                                   op0=ALU.mult, op1=ALU.add))
            ch.mark(nc.vector.tensor_scalar(powin[:, 1, :], var[:, :], float(D), None, ALU.mult))
            pows[0] += 1
            nc.vector.tensor_scalar(powin[:, 0, :], var[:, :], LN_EPS, None, ALU.add).then_inc(pow_asked, 1)

        def normalise(dve, ch, dst, src, which=0):
            b3 = [P, NT, D]
            ch.link(nc.vector.tensor_tensor(dst, src, bcast(mean[:, :].unsqueeze(2), b3), ALU.subtract))
            dve.wait_ge(pow_done, pows[0])
            ch.link(nc.vector.tensor_tensor(dst, dst, bcast(powout[:, which, :].unsqueeze(2), b3), ALU.mult))

        def pool_pow(pool, k):
            pool.wait_ge(pow_asked, k)
            nc.gpsimd.tensor_tensor(powout[:, :, :], powin[:, :, :], minus_half[:, :, :],
                                    ALU.pow).then_inc(pow_done, 1)

        def transpose_in(pe, src, ready, value, done, banks=(4, 5, 6, 7)):
            pe.wait_ge(ready, value)
            for c, b in enumerate(banks):
                for i in range(TPC):
                    mm = nc.tensor.transpose(bank[:, b, i * P:(i + 1) * P], src[:, c * TPC + i, :], ident[:, :])
                mm.then_inc(done, 1)

        slots, wn_f, e1, e2, pm, acc, yT, upd, wraw, wT, biasb, dead_f = carve(
            4 * N // 2, NT * D, 2 * CH, 3 * CH, 3 * CH, CH, CH, CH, D, D, D, N // 2)
        dead = dead_f.bitcast(BF16)
        slot = slots.bitcast(BF16).rearrange("p (s n) -> p s n", s=TPC)
        wn = wn_f.rearrange("p (t d) -> p t d", t=NT)
        e1 = e1.rearrange("p (s n) -> p s n", s=2)
        e2 = e2.rearrange("p (s n) -> p s n", s=3)
        pm = pm.rearrange("p (s n) -> p s n", s=3)
        bs = sb("bs", [P, 1])
        rs = sb("rs", [P, TPC])

        ld_x, ld_w, ld_b, ld_bias = sem("ld_x"), sem("ld_w"), sem("ld_b"), sem("ld_bias")
        adj_ld = [sem(f"adj_ld{i}") for i in range(TPC)]
        consts, identities = sem("consts"), sem("identities")
        ach_v, ach_a, ach_p = sem("ach_v"), sem("ach_a"), sem("ach_p")
        xn_ready = sem("xn_ready")
        wn_ready, wnT_done, wnT_out, wT_done, wT_out = (sem(s) for s in (
            "wn_ready", "wnT_done", "wnT_out", "wT_done", "wT_out"))
        tr_done, tr_free, slot_summed = sem("tr_done"), sem("tr_free"), sem("slot_summed")
        s_done, s_free, exp_done, pm_ready, pm_used = (sem(s) for s in (
            "s_done", "s_free", "exp_done", "pm_ready", "pm_used"))
        yT_out, acc_done, sum_done, proj_done, x_done = (sem(s) for s in (
            "yT_out", "acc_done", "sum_done", "proj_done", "x_done"))
        adj_rows = adj.rearrange("(t p) n -> t p n", p=P)

        with nc.Block() as block:
            @block.sync
            def _(sp):
                sp.dma_start(res[:, :, :], x.rearrange("(t p) d -> p t d", p=P)).then_inc(ld_x, 16)
                sp.dma_start(wraw, L0_gnn_W).then_inc(ld_w, 16)
                sp.dma_start(bs[:, :], bcast(L0_gnn_b.rearrange("(a n) -> a n", a=1), [P, 1])).then_inc(ld_b, 16)
                sp.dma_start(biasb, bcast(L0_gnn_bias.rearrange("(a n) -> a n", a=1), [P, D])).then_inc(ld_bias, 16)

            @block.gpsimd
            def _(pool):
                for s in range(TPC):
                    pool.dma_start(slot[:, s, :], adj_rows[s]).then_inc(adj_ld[s], 16)
                ch = Chain(pool, ach_p)
                nc.gpsimd.memset(minus_half[:, :, :], -0.5).then_inc(consts, 1)
                nc.gpsimd.memset(ones[:, :], 1.0).then_inc(consts, 1)
                ch.mark(nc.gpsimd.memset(ident[:, :], 0.0))
                ch.link(nc.gpsimd.memset(identb[:, :], 0.0))
                for m in (ident, identb):
                    nc.gpsimd.affine_select(out=m[:, :], in_=m[:, :], compare_op=ALU.not_equal, fill=1.0, base=0,
                                            pattern=[[-1, P]], channel_multiplier=1).then_inc(identities, 1)
                pool.wait_ge(consts, 1)
                pool_pow(pool, 1)
                with pool.Fori(1, NC) as c:
                    for s in range(TPC):
                        pool.wait_ge(tr_done, c * 8 + (2 * s - 6))
                        pool.wait_ge(slot_summed, c * TPC + (s - 2))
                        pool.dma_start(slot[:, s, :], adj_rows[bass.ds(c * TPC + s, 1)].rearrange("a p n -> (a p) n")
                                       ).then_inc(adj_ld[s], 16)

            @block.vector
            def _(dve):
                ch = Chain(dve, ach_v)
                dve.sem_inc(tr_free, 2)
                dve.sem_inc(pm_ready, 3)
                dve.wait_ge(ld_x, 16)
                moments(dve, ch, res)
                normalise(dve, ch, wn, res[:, :, :], 1)
                nc.vector.tensor_copy(rs[:, 3:4], wn[:, 0, 0:1]).then_inc(wn_ready, 1)
                normalise(dve, ch, xn[:, :, :], res[:, :, :], 0)
                nc.vector.tensor_copy(rs[:, 2:3], xn[:, 0, 0:1]).then_inc(xn_ready, 1)
                dve.wait_ge(ld_bias, 16)
                ch.link(nc.vector.tensor_tensor(res[:, :, :], res[:, :, :],
                                                bcast(biasb.unsqueeze(1), [P, NT, D]), ALU.add))
                for c in range(0, NC, 2):
                    dve.wait_ge(wnT_done, c + 1)
                    nc.vector.tensor_copy(xnT[:, c * CH:(c + 1) * CH], bank[:, 4 + c, :]).then_inc(wnT_out, 1)
                dve.wait_ge(wT_done, 1)
                nc.vector.tensor_copy(wT, bank[:, 0, 0:D]).then_inc(wT_out, 1)

                with dve.Fori(0, NC) as c:
                    ch.enter(c, 2)
                    for s in range(TPC):
                        for h in range(2):
                            dve.wait_ge(tr_done, c * 8 + (2 * s + h + 1))
                            nc.vector.tensor_copy(
                                adjT[:, 8 * h:8 * h + 8, bass.ds(c * CH + s * P, P)],
                                bankb[:, 5 + h, :].rearrange("p (a b) -> p a b", a=8)).then_inc(tr_free, 1)
                    dve.wait_ge(tr_free, c * 8 + 10)
                    for jt in range(NT):
                        dve.wait_ge(exp_done, c * NT + (jt + 1))
                        dve.wait_ge(pm_used, c * NT + (jt + 1))
                        nc.vector.tensor_tensor(pm[:, jt % 3, :], e2[:, jt % 3, :],
                                                adjT[:, jt, bass.ds(c * CH, CH)], ALU.mult).then_inc(pm_ready, 1)
                        dve.wait_ge(pm_ready, c * NT + (jt + 4))
                        if jt == 0:
                            dve.wait_ge(sum_done, c + 1)
                            nc.vector.tensor_copy(acc, pm[:, 0, :]).then_inc(acc_done, 1)
                        else:
                            dve.wait_ge(acc_done, c * NT + jt)
                            nc.vector.tensor_tensor(acc, acc, pm[:, jt % 3, :], ALU.add).then_inc(acc_done, 1)
                    dve.wait_ge(sum_done, c + 2)
                    ch.link(nc.vector.reciprocal(rs[:, :], bank[:, 3, 0:TPC]))
                    dve.wait_ge(proj_done, c + 2)
                    ch.link(nc.vector.tensor_tensor(upd.rearrange("p (t d) -> p t d", t=TPC),
                                                    bank[:, 4, :].rearrange("p (t d) -> p t d", t=TPC),
                                                    bcast(rs[:, :].unsqueeze(2), [P, TPC, D]), ALU.mult))
                    r = resflat[:, bass.ds(c * CH, CH)]
                    nc.vector.tensor_tensor(r, r, upd, ALU.add).then_inc(x_done, 1)
                    ch.leave(NC)
                dve.wait_ge(x_done, NC)

            @block.scalar
            def _(act):
                ch = Chain(act, ach_a)
                act.wait_ge(ld_b, 16)
                act.sem_inc(s_free, 2)
                act.sem_inc(slot_summed, 1)
                act.sem_inc(yT_out, 1)
                ch.link(nc.scalar.activation(bs[:, :], bs[:, :], ACT.Copy, scale=1.0 / 8.0))
                for c in range(1, NC, 2):
                    act.wait_ge(wnT_done, c + 1)
                    nc.scalar.activation(xnT[:, c * CH:(c + 1) * CH], bank[:, 4 + c, :],
                                         ACT.Copy).then_inc(wnT_out, 1)
                with act.Fori(0, NC) as c:
                    for jt in range(NT):
                        act.wait_ge(s_done, c * NT + (jt + 1))
                        nc.scalar.activation(e1[:, jt % 2, :], bank[:, jt % 2, :], ACT.Tanh,
                                             scale=bs[:, 0:1]).then_inc(s_free, 1)
                        act.wait_ge(s_free, c * NT + (jt + 3))
                        act.wait_ge(pm_ready, c * NT + (jt + 1))
                        nc.scalar.activation(e2[:, jt % 3, :], e1[:, jt % 2, :], ACT.Exp,
                                             scale=8.0).then_inc(exp_done, 1)
                        if jt % TPC == 0:
                            s = jt // TPC
                            act.wait_ge(adj_ld[s], c * 16 + 16)
                            act.wait_ge(slot_summed, c * TPC + s + 1)
                            nc.scalar.activation(dead, slot[:, s, :], ACT.Copy,
                                                 accum_out=rowsum[:, bass.ds(c * TPC + s, 1)]
                                                 ).then_inc(slot_summed, 1)
                    act.wait_ge(pm_used, c * NT + (NT + 3))
                    act.wait_ge(proj_done, c + 1)
                    nc.scalar.activation(yT, bank[:, 2, :], ACT.Copy).then_inc(yT_out, 1)

            @block.tensor
            def _(pe):
                pe.wait_ge(identities, 2)
                pe.wait_ge(consts, 2)
                transpose_in(pe, wn, wn_ready, 1, wnT_done)
                pe.wait_ge(ld_w, 16)
                nc.tensor.transpose(bank[:, 0, 0:D], wraw, ident[:, :]).then_inc(wT_done, 1)
                pe.sem_inc(pm_used, 3)
                pe.sem_inc(sum_done, 1)
                pe.sem_inc(proj_done, 1)
                pe.wait_ge(wT_out, 1)
                pe.wait_ge(wnT_out, NC)
                pe.wait_ge(xn_ready, 1)
                with pe.Fori(0, NC) as c:
                    for s in range(TPC):
                        pe.wait_ge(adj_ld[s], c * 16 + 16)
                        for h in range(2):
                            pe.wait_ge(tr_free, c * 8 + (2 * s + h + 1))
                            for b in range(8):
                                j = (8 * h + b) * P
                                mm = nc.tensor.transpose(bankb[:, 5 + h, b * P:(b + 1) * P], slot[:, s, j:j + P],
                                                         identb[:, :])
                            mm.then_inc(tr_done, 1)

                    def score(jt):
                        pe.wait_ge(s_free, c * NT + (jt + 1))
                        nc.tensor.matmul(bank[:, jt % 2, :], xnT[:, jt * P:(jt + 1) * P], xnT[:, bass.ds(c * CH, CH)],
                                         start=True, stop=True).then_inc(s_done, 1)

                    score(0)
                    score(1)
                    pe.wait_ge(yT_out, c + 1)
                    for jt in range(NT):
                        if jt + 2 < NT:
                            score(jt + 2)
                        pe.wait_ge(pm_ready, c * NT + (jt + 4))
                        mm = nc.tensor.matmul(bank[:, 2, :], xn[:, jt, :], pm[:, jt % 3, :], start=(jt == 0),
                                              stop=(jt == NT - 1))
                        mm.then_inc(pm_used, 1)
                    pe.wait_ge(acc_done, c * NT + NT)
                    for t in range(TPC):
                        mm = nc.tensor.matmul(bank[:, 3, t:t + 1], acc[:, t * P:(t + 1) * P], ones[:, 0:1],
                                              start=True, stop=True)
                    mm.then_inc(sum_done, 1)
                    pe.wait_ge(yT_out, c + 2)
                    for t in range(TPC):
                        mm = nc.tensor.matmul(bank[:, 4, t * P:(t + 1) * P], yT[:, t * P:(t + 1) * P], wT,
                                              start=True, stop=True)
                    mm.then_inc(proj_done, 1)

        finish_early = sem("finish_early")
        if stop_after == "A":
            with nc.Block() as block:
                @block.sync
                def _(sp):
                    sp.dma_start(out.rearrange("(t p) d -> p t d", p=P), res[:, :, :]).then_inc(finish_early, 16)
                    sp.wait_ge(finish_early, 16)
            return

        E, H = L0_ffn_w1.shape[0], L0_ffn_w1.shape[2]
        HC = H // P
        UN = NC * HC
        (wb1, wb2, wb3, dispB, sil, sild, gb, moeT, gl, m8, oh1, oh2, gatew, gateb, gsm, dispT, iotaf, zerob) = carve(
            2 * H, 2 * H, 2 * HC * D, 2 * N, 2 * CH, 2 * CH, 2 * CH, N, NT * E, NT * 8, NT * E, NT * E, E, E,
            8 * NT, N, E, P // 2)
        wb1 = wb1.rearrange("p (k h) -> p k h", k=2)
        wb2 = wb2.rearrange("p (k h) -> p k h", k=2)
        wb3 = wb3.rearrange("p (k c d) -> p k c d", k=2, c=HC)
        dispB = dispB.rearrange("p (k n) -> p k n", k=2)
        sil, sild = (v.rearrange("p (k n) -> p k n", k=2) for v in (sil, sild))
        gb = gb.rearrange("p (k n) -> p k n", k=2)
        gl, oh1, oh2 = (v.rearrange("p (t e) -> p t e", t=NT) for v in (gl, oh1, oh2))
        m8 = m8.rearrange("p (t e) -> p t e", t=NT)
        gsm = gsm.rearrange("p (k t) -> p k t", k=8)
        zerob = zerob.bitcast(BF16)
        i8 = sb("i8", [P, NT, 8], U32)
        iotai = sb("iotai", [P, 16], I32)
        disp_dram = nc.dram_tensor("disp_scratch", (E, N), F32).ap()

        ld_g, iota_done, bch_v, bch_a = sem("ld_g"), sem("iota_done"), sem("bch_v"), sem("bch_a")
        (b_xn, b_xT_done, b_xT_out, gl_done, l21, e21, disp_ready, dT_done, dT_out, disp_st) = (sem("b_" + s) for s in (
            "xn", "xT_done", "xT_out", "gl_done", "l21", "e21", "disp_ready", "dT_done", "dT_out", "disp_st"))
        w_ld = [sem(f"w_ld{k}") for k in range(2)]
        (h1_done, h2_done, sil_done, sild_done, g_ready, g_used, moe_out, moeT_done, b_x) = (
            sem("b_" + s) for s in ("h1_done", "h2_done", "sil_done", "sild_done", "g_ready", "g_used",
                                    "moe_out", "moeT_done", "x_done"))
        zeroed = sem("zeroed")

        def copy_xT(dve_or_act, done, outs, odd, eng):
            for c in range(odd, NC, 2):
                eng.wait_ge(done, c + 1)
                dst, src = xnT[:, c * CH:(c + 1) * CH], bank[:, 4 + c, :]
                if odd:
                    nc.scalar.activation(dst, src, ACT.Copy).then_inc(outs, 1)
                else:
                    nc.vector.tensor_copy(dst, src).then_inc(outs, 1)

        with nc.Block() as block:
            @block.sync
            def _(sp):
                sp.dma_start(gatew, L0_ffn_gate_w).then_inc(ld_g, 16)
                sp.dma_start(gateb, bcast(L0_ffn_gate_b.rearrange("(a n) -> a n", a=1), [P, E])).then_inc(ld_g, 16)
                sp.wait_ge(dT_out, NC)
                sp.dma_start(disp_dram, dispT[0:E, :]).then_inc(disp_st, 16)
                sp.wait_ge(disp_st, 16)
                with sp.Fori(0, E // 2) as i:
                    for k in range(2):
                        sp.wait_ge(g_used, i * 2 * UN + (k * UN + 1))
                        e1_ = bass.ds(i * 2 + k, 1)
                        sp.dma_start(wb1[:, k, :], L0_ffn_w1[e1_].rearrange("a p h -> (a p) h")).then_inc(w_ld[k], 16)
                        sp.dma_start(wb2[:, k, :], L0_ffn_w2[e1_].rearrange("a p h -> (a p) h")).then_inc(w_ld[k], 16)
                        sp.dma_start(wb3[:, k, :, :], L0_ffn_w3[e1_].rearrange("a (c p) d -> (a p) c d", p=P)
                                     ).then_inc(w_ld[k], 16)
                        sp.dma_start(dispB[:, k, :], bcast(disp_dram[e1_, :], [P, N])).then_inc(w_ld[k], 16)

            @block.gpsimd
            def _(pool):
                nc.gpsimd.iota(iotai[:, :], pattern=[[1, 16]], base=0, channel_multiplier=0).then_inc(iota_done, 1)
                nc.gpsimd.memset(zerob, 0.0).then_inc(iota_done, 1)
                pool_pow(pool, 2)

            @block.vector
            def _(dve):
                ch = Chain(dve, bch_v)
                moments(dve, ch, res)
                normalise(dve, ch, xn[:, :, :], res[:, :, :], 0)
                nc.vector.tensor_copy(tmp16[:, 0:1], xn[:, 0, 0:1]).then_inc(b_xn, 1)
                copy_xT(None, b_xT_done, b_xT_out, 0, dve)
                dve.wait_ge(iota_done, 1)
                ch.mark(nc.vector.tensor_copy(iotaf, iotai[:, 0:E]))
                dve.wait_ge(gl_done, 1)
                dve.wait_ge(ld_g, 32)
                ch.link(nc.vector.tensor_tensor(gl, bank[:, 0, 0:NT * E].rearrange("p (t e) -> p t e", t=NT),
                                                bcast(gateb.unsqueeze(1), [P, NT, E]), ALU.add))
                for t in range(NT):
                    ch.mark(nc.vector.max(m8[:, t, :], gl[:, t, :]))
                ch.sync()
                nc.vector.tensor_tensor(gsm[:, 0, :], m8[:, :, 1], m8[:, :, 0], ALU.subtract).then_inc(l21, 1)
                for t in range(NT):
                    ch.mark(nc.vector.max_index(i8[:, t, :], m8[:, t, :], gl[:, t, :]))
                ch.sync()
                ch.mark(nc.vector.tensor_copy(gsm[:, 4, :], i8[:, :, 0]))
                ch.mark(nc.vector.tensor_copy(gsm[:, 5, :], i8[:, :, 1]))
                dve.wait_ge(e21, 1)
                ch.link(nc.vector.tensor_scalar(gsm[:, 2, :], gsm[:, 1, :], 1.0, None, ALU.add))
                ch.link(nc.vector.reciprocal(gsm[:, 2, :], gsm[:, 2, :]))
                ch.link(nc.vector.tensor_tensor(gsm[:, 3, :], gsm[:, 1, :], gsm[:, 2, :], ALU.mult))
                b3 = [P, NT, E]
                for o, w, q in ((oh1, 2, 4), (oh2, 3, 5)):
                    ch.link(nc.vector.tensor_tensor(o, bcast(gsm[:, q, :].unsqueeze(2), b3),
                                                    bcast(iotaf.unsqueeze(1), b3), ALU.is_equal))
                    ch.link(nc.vector.tensor_tensor(o, o, bcast(gsm[:, w, :].unsqueeze(2), b3), ALU.mult))
                nc.vector.tensor_tensor(oh1, oh1, oh2, ALU.add).then_inc(disp_ready, 1)
                for c in range(NC):
                    dve.wait_ge(dT_done, c + 1)
                    nc.vector.tensor_copy(dispT[0:E, c * CH:(c + 1) * CH], bank[0:E, 4 + c, :]).then_inc(dT_out, 1)
                dve.sem_inc(g_ready, 2)
                with dve.Fori(0, E // 2) as i:
                    for k in range(2):
                        dve.wait_ge(w_ld[k], i * 64 + 64)
                        for v in range(UN):
                            u = k * UN + v
                            c = v // HC
                            dve.wait_ge(sil_done, i * 2 * UN + (u + 1))
                            nc.vector.tensor_tensor(sild[:, u % 2, :], sil[:, u % 2, :],
                                                    dispB[:, k, c * CH:(c + 1) * CH], ALU.mult).then_inc(sild_done, 1)
                            dve.wait_ge(sild_done, i * 2 * UN + (u + 1))
                            dve.wait_ge(h2_done, i * 2 * UN + (u + 1))
                            dve.wait_ge(g_used, i * 2 * UN + (u + UN))
                            nc.vector.tensor_tensor(gb[:, u % 2, :], sild[:, u % 2, :], bank[:, 2 * (u % 2) + 1, :],
                                                    ALU.mult).then_inc(g_ready, 1)
                for c in range(0, NC, 2):
                    dve.wait_ge(g_used, E * UN + (UN + 1))
                    nc.vector.tensor_copy(moeT[:, c * CH:(c + 1) * CH], bank[:, 4 + c, :]).then_inc(moe_out, 1)
                for c in range(NC):
                    dve.wait_ge(moeT_done, c + 1)
                    r = resflat[:, c * CH:(c + 1) * CH]
                    nc.vector.tensor_tensor(r, r, bank[:, c, :], ALU.add).then_inc(b_x, 1)
                dve.wait_ge(b_x, NC)

            @block.scalar
            def _(act):
                copy_xT(None, b_xT_done, b_xT_out, 1, act)
                act.wait_ge(l21, 1)
                nc.scalar.activation(gsm[:, 1, :], gsm[:, 0, :], ACT.Exp).then_inc(e21, 1)
                with act.Fori(0, E // 2) as i:
                    for u in range(2 * UN):
                        act.wait_ge(h1_done, i * 2 * UN + (u + 1))
                        act.wait_ge(g_ready, i * 2 * UN + (u + 1))
                        nc.scalar.activation(sil[:, u % 2, :], bank[:, 2 * (u % 2), :], ACT.Silu).then_inc(sil_done, 1)
                for c in range(1, NC, 2):
                    act.wait_ge(g_used, E * UN + (UN + 1))
                    nc.scalar.activation(moeT[:, c * CH:(c + 1) * CH], bank[:, 4 + c, :], ACT.Copy
                                         ).then_inc(moe_out, 1)

            @block.tensor
            def _(pe):
                transpose_in(pe, xn[:, :, :], b_xn, 1, b_xT_done)
                pe.wait_ge(b_xT_out, NC)
                pe.wait_ge(ld_g, 32)
                for t in range(NT):
                    mm = nc.tensor.matmul(bank[:, 0, t * E:(t + 1) * E], xnT[:, t * P:(t + 1) * P], gatew,
                                          start=True, stop=True)
                mm.then_inc(gl_done, 1)
                pe.wait_ge(disp_ready, 1)
                for c in range(NC):
                    for t in range(TPC):
                        mm = nc.tensor.transpose(bank[0:E, 4 + c, t * P:(t + 1) * P], oh1[:, c * TPC + t, :], ident[:, :])
                    mm.then_inc(dT_done, 1)
                pe.sem_inc(g_used, UN + 1)
                pe.wait_ge(dT_out, NC)
                pe.wait_ge(iota_done, 2)
                for c in range(NC):
                    nc.tensor.matmul(bank[:, 4 + c, :], zerob, adjT[:, 0, 0:CH], start=True, stop=False,
                                     skip_group_check=True)

                with pe.Fori(0, E // 2) as i:
                    def up(u):
                        k, v = divmod(u, UN)
                        c, hc = divmod(v, HC)
                        if v == 0:
                            pe.wait_ge(w_ld[k], i * 64 + 64)
                        pe.wait_ge(g_ready, i * 2 * UN + (u + 1))
                        for w, b, done in ((wb1, 0, h1_done), (wb2, 1, h2_done)):
                            nc.tensor.matmul(bank[:, 2 * (u % 2) + b, :], w[:, k, hc * P:(hc + 1) * P],
                                             xnT[:, c * CH:(c + 1) * CH], start=True, stop=True).then_inc(done, 1)

                    def down(u):
                        k, v = divmod(u, UN)
                        c, hc = divmod(v, HC)
                        pe.wait_ge(g_ready, i * 2 * UN + (u + 3))
                        nc.tensor.matmul(bank[:, 4 + c, :], wb3[:, k, hc, :], gb[:, u % 2, :], start=False, stop=False,
                                         skip_group_check=True).then_inc(g_used, 1)

                    up(0)
                    for u in range(2 * UN):
                        if u + 1 < 2 * UN:
                            up(u + 1)
                        down(u)
                pe.wait_ge(moe_out, NC)
                for c in range(NC):
                    for t in range(TPC):
                        mm = nc.tensor.transpose(bank[:, c, t * P:(t + 1) * P],
                                                 moeT[:, c * CH + t * P:c * CH + (t + 1) * P], ident[:, :])
                    mm.then_inc(moeT_done, 1)

        if stop_after == "B":
            with nc.Block() as block:
                @block.sync
                def _(sp):
                    sp.dma_start(out.rearrange("(t p) d -> p t d", p=P), res[:, :, :]).then_inc(finish_early, 16)
                    sp.wait_ge(finish_early, 16)
            return
        DA = L1_gnn_W1.shape[0]
        STEPS = L1_gnn_U1.shape[0]
        TOP_P = 0.9
        G = 2
        NG = NT // G
        GW = G * P
        SEG, NSEG = P, N // P
        LEAST_BITS = (127 - 15) << 23
        RANGE_BITS = 15 << 23
        COARSE = (0, 6)
        ROUNDS = (5, 5)
        EXACT = 40
        (prob, mk, MT) = carve(2 * G * N, G * N, NT * GW)
        prob = prob.rearrange("p (b s n) -> p b s n", b=2, s=G)
        mk = mk.rearrange("p (s n) -> p s n", s=G)
        raw = prob[:, 1, 0, 0:P]
        ranks = MT[:, 0:N]
        MT = MT.rearrange("p (j i) -> p j i", j=NT)
        ties = xnT
        waste = xnT[:, :].bitcast(BF16).rearrange("p (s n) -> p s n", s=G)
        MARKS = (60, 150)
        chain_v = [0]
        xa2 = sb("xa2", [P, NT, D])
        xf2 = sb("xf2", [P, NT, D])
        hacc = sb("hacc", [P, NT, D])
        parts = sb("parts", [P, 3, NT, D], BF16)
        kq = sb("kq", [P, N])
        qst = sb("qst", [DA, 2, GW])
        GTs = sb("GTs", [P, GW])
        ZTs = sb("ZTs", [P, GW])
        UT = sb("UT", [P, 2 * STEPS, D])
        wkq = sb("wkq", [P, P])
        cand = sb("cand", [P, G, 8 * NSEG])
        top = sb("top", [P, G, 8 * max(ROUNDS)])
        cum = sb("cum", [P, G, 8 * max(ROUNDS)])
        rm8 = sb("rm8", [P, 8])
        negm = sb("negm", [P, G])
        Z = sb("Z", [P, 2, G])
        st = sb("st", [P, 16, G])
        (T_, ZR, L_, TB, F_, GE, Q_, FH, V_, SM, BAD, LO, HI, THETA, BAD2, LAST) = range(16)
        fsc = sb("fsc", [P, 2, G])
        rinv = sb("rinv", [P, NT])
        flag = sb("flag", [P, 32])
        flagT = sb("flagT", [P, 32])
        any4 = sb("any4", [P, 1])
        pause = sb("pause", [P, 1])
        any4i = sb("any4i", [P, 1], I32)

        def S(k):
            return st[:, k, :]

        def S1(k, s):
            return st[:, k, s:s + 1]

        def names(prefix, *n):
            return [sem(prefix + "_" + x) for x in n]

        (c_ld, c_wt_done, c_wt_out, c_xn, c_xT_done, c_xT_out, c_kq_done, c_kq_out, c_m_done, c_m_out) = names(
            "c", "ld", "wt_done", "wt_out", "xn", "xT_done", "xT_out", "kq_done", "kq_out", "m_done", "m_out")
        (q_ready, l_done, nm_ready, p_ready, m_ready, tq_done, mt_out, pv_done, rx_done, gts_out, zts_out, post_done,
         post_v, post_a, split_done, cch_v, cch_p, raw_ld, raw_used) = names(
            "c", "q_ready", "l_done", "nm_ready", "p_ready", "m_ready", "tq_done", "mt_out", "pv_done", "rx_done",
            "gts_out", "zts_out", "post_done", "post_v", "post_a", "split_done", "ch_v", "ch_p", "raw_ld", "raw_used")

        with nc.Block() as block:
            @block.sync
            def _(sp):
                sp.dma_start(raw[0:DA, :], L1_gnn_W3).then_inc(c_ld, 16)
                sp.dma_start(GTs[0:DA, 0:P], L1_gnn_W1).then_inc(c_ld, 16)
                sp.dma_start(GTs[0:DA, P:P + DA], L1_gnn_W2).then_inc(c_ld, 16)
                for n in range(STEPS):
                    sp.dma_start(prob[:, 0, 0, 2 * n * D:(2 * n + 1) * D], L1_gnn_U1[n]).then_inc(c_ld, 16)
                    sp.dma_start(prob[:, 0, 0, (2 * n + 1) * D:(2 * n + 2) * D], L1_gnn_U2[n]).then_inc(c_ld, 16)

            @block.gpsimd
            def _(pool):
                ch = Chain(pool, cch_p)
                for t in range(NT):
                    d = adjT[:, t, t * P:(t + 1) * P]
                    ch.mark(nc.gpsimd.tensor_tensor(d, d, identb[:, :], ALU.add))
                ch.mark(nc.gpsimd.memset(flag[:, :], 0.0))
                pool_pow(pool, 3)
                ch.sync()

            @block.vector
            def _(dve):
                ch = Chain(dve, cch_v)
                moments(dve, ch, res)
                ch.link(nc.vector.tensor_scalar(rinv[:, :], rowsum[:, :], 1.0, None, ALU.add))
                ch.link(nc.vector.reciprocal(rinv[:, :], rinv[:, :]))
                normalise(dve, ch, xn[:, :, :], res[:, :, :], 0)
                ch.link(nc.vector.tensor_copy(hacc[:, :, :], xn[:, :, :]))
                dve.wait_ge(c_wt_done, 1)
                nc.vector.tensor_copy(wkq[:, 0:DA], bank[:, 0, 0:DA]).then_inc(c_wt_out, 1)
                dve.wait_ge(c_wt_done, 2)
                nc.vector.tensor_copy(raw[0:DA, 0:DA], bank[0:DA, 1, 0:DA]).then_inc(c_wt_out, 1)
                dve.wait_ge(c_m_done, 1)
                nc.vector.tensor_copy(wkq[:, DA:2 * DA], bank[:, 2, 0:DA]).then_inc(c_m_out, 1)
                dve.wait_ge(c_wt_done, 3)
                nc.vector.tensor_copy(UT[:, :, :], bank[:, 3, :].rearrange("p (k d) -> p k d", k=2 * STEPS)
                                      ).then_inc(c_m_out, 1)
                dve.wait_ge(c_m_out, 2)
                chain_v[0] = ch.n

            @block.tensor
            def _(pe):
                pe.wait_ge(c_ld, 16 * (3 + 2 * STEPS))
                nc.tensor.transpose(bank[:, 0, 0:DA], raw[0:DA, :], ident[0:DA, 0:DA]).then_inc(c_wt_done, 1)
                nc.tensor.transpose(bank[0:DA, 1, 0:DA], GTs[0:DA, P:P + DA], ident[0:DA, 0:DA]).then_inc(c_wt_done, 1)
                for k in range(2 * STEPS):
                    mm = nc.tensor.transpose(bank[:, 3, k * D:(k + 1) * D], prob[:, 0, 0, k * D:(k + 1) * D], ident[:, :])
                mm.then_inc(c_wt_done, 1)
                pe.wait_ge(c_wt_out, 2)
                nc.tensor.matmul(bank[:, 2, 0:DA], GTs[0:DA, 0:P], raw[0:DA, 0:DA], start=True, stop=True
                                 ).then_inc(c_m_done, 1)

        def step_block(n):
            base = n * NG
            xsrc, fsrc = (xn, xn) if n == 0 else (xa2, xf2)
            last = n == STEPS - 1
            R8 = 8 * ROUNDS[n]

            with nc.Block() as block:
                @block.gpsimd
                def _(pool):
                    ch = Chain(pool, cch_p)
                    ch.n = NT + 1 + 5 * n
                    f, r = fsrc[:, :, :], xf2[:, :, :]
                    ch.link(nc.gpsimd.tensor_copy(parts[:, 0, :, :], f))
                    ch.link(nc.gpsimd.tensor_tensor(r, f, parts[:, 0, :, :], ALU.subtract))
                    ch.link(nc.gpsimd.tensor_copy(parts[:, 1, :, :], r))
                    ch.link(nc.gpsimd.tensor_tensor(r, r, parts[:, 1, :, :], ALU.subtract))
                    ch.link(nc.gpsimd.tensor_copy(parts[:, 2, :, :], r))
                    pool.sem_inc(split_done, 1)

                @block.vector
                def _(dve):
                    ch = Chain(dve, cch_v)
                    ch.n = chain_v[0]
                    if n == 0:
                        dve.sem_inc(m_ready, 2)
                        dve.sem_inc(post_v, 1)
                    for c in range(0, NC, 2):
                        dve.wait_ge(c_xT_done, n * NC + c + 1)
                        nc.vector.tensor_copy(xnT[:, c * CH:(c + 1) * CH], bank[:, 4 + c, :]).then_inc(c_xT_out, 1)
                    for c in range(0, NC, 2):
                        dve.wait_ge(c_kq_done, n * NC + c + 1)
                        nc.vector.tensor_copy(kq[:, c * CH:(c + 1) * CH], bank[:, c, :]).then_inc(c_kq_out, 1)

                    def row_max(gg, s):
                        dve.wait_ge(l_done, gg * G + (s + 1))
                        ch.mark(nc.vector.tensor_copy(pause[:, :], rinv[:, 0:1]))
                        ch.link(nc.vector.max(rm8[:, :], bank[:, 0:4, :].rearrange("p b n -> p (b n)")))
                        nc.vector.tensor_scalar(negm[:, s:s + 1], rm8[:, 0:1], -1.0, None,
                                                ALU.mult).then_inc(nm_ready, 1)

                    def cut_ties(b, sync):
                        sync()
                        for s in range(G):
                            sync(nc.vector.scalar_tensor_tensor(
                                out=mk[:, s, :], in0=prob[:, b, s, :], scalar=S1(V_, s), in1=prob[:, b, s, :],
                                op0=ALU.is_gt, op1=ALU.mult, accum_out=S1(F_, s)), wait=False)
                        sync()
                        sync(nc.vector.tensor_tensor(S(THETA), S(T_), S(V_), ALU.add), wait=False)
                        for s in range(G):
                            sync(nc.vector.tensor_scalar(ties[:, :], prob[:, b, s, :], S1(V_, s), S1(V_, s),
                                                         ALU.is_equal, ALU.mult))
                            sync(nc.vector.tensor_tensor_scan(ranks, ties[:, :], ties[:, :], S1(F_, s), ALU.add,
                                                              ALU.max))
                            sync(nc.vector.tensor_copy(S1(LAST, s), ranks[:, N - 1:N]), wait=False)
                            sync(nc.vector.scalar_tensor_tensor(
                                out=ties[:, :], in0=ranks, scalar=S1(THETA, s), in1=ties[:, :],
                                op0=ALU.is_lt, op1=ALU.mult, accum_out=S1(SM, s)))
                            sync(nc.vector.tensor_tensor(mk[:, s, :], mk[:, s, :], ties[:, :], ALU.add))
                        sync(nc.vector.tensor_tensor(S(SM), S(SM), S(F_), ALU.add))

                    def linked(ins=None, wait=True):
                        if ins is not None:
                            ch.mark(ins)
                        if wait:
                            ch.sync()

                    def drained(ins=None, wait=True):
                        if wait:
                            dve.drain()

                    def exact(b):
                        nc.vector.memset(S(LO), 2.0 ** -15)
                        nc.vector.memset(S(HI), 1.0)
                        dve.drain()
                        with dve.Fori(0, EXACT) as _i:
                            nc.vector.tensor_tensor(S(TB), S(LO), S(HI), ALU.add)
                            dve.drain()
                            nc.vector.tensor_scalar(S(TB), S(TB), 0.5, None, ALU.mult)
                            dve.drain()
                            for s in range(G):
                                nc.vector.scalar_tensor_tensor(
                                    out=mk[:, s, :], in0=prob[:, b, s, :], scalar=S1(TB, s), in1=prob[:, b, s, :],
                                    op0=ALU.is_gt, op1=ALU.mult, accum_out=S1(F_, s))
                            dve.drain()
                            nc.vector.tensor_tensor(S(GE).bitcast(I32), S(F_), S(T_), ALU.is_ge)
                            nc.vector.tensor_tensor(S(Q_).bitcast(I32), S(F_), S(T_), ALU.is_lt)
                            dve.drain()
                            nc.vector.copy_predicated(S(LO), S(GE).bitcast(I32), S(TB))
                            nc.vector.copy_predicated(S(HI), S(Q_).bitcast(I32), S(TB))
                            dve.drain()
                        nc.vector.tensor_copy(S(V_), S(HI))
                        dve.drain()

                    def post(gg, tile, pb):
                        dve.wait_ge(post_done, gg + 1)
                        for s in range(G):
                            hs = hacc[:, bass.ds(tile + s, 1), :].rearrange("p a d -> p (a d)")
                            ch.mark(nc.vector.scalar_tensor_tensor(
                                out=hs, in0=bank[:, 4, GW + s * P:GW + (s + 1) * P],
                                scalar=rinv[:, bass.ds(tile + s, 1)], in1=hs, op0=ALU.mult, op1=ALU.add))
                        ch.sync()
                        for s in range(G):
                            hs = hacc[:, bass.ds(tile + s, 1), :].rearrange("p a d -> p (a d)")
                            ch.mark(nc.vector.scalar_tensor_tensor(
                                out=hs, in0=bank[:, 7, GW + s * P:GW + (s + 1) * P],
                                scalar=fsc[:, pb, s:s + 1], in1=hs, op0=ALU.mult, op1=ALU.add))
                        ch.sync()
                        dve.sem_inc(post_v, 1)

                    def group(g, b, prefetch, after):
                        gg = g + base
                        dve.wait_ge(p_ready, gg * G + G)
                        dve.wait_ge(m_ready, gg + 2)
                        if prefetch:
                            row_max(gg + 1, 0)
                        ch.mark(nc.vector.tensor_scalar(S(T_), Z[:, b, :], TOP_P, None, ALU.mult))
                        ch.link(nc.vector.reciprocal(S(ZR), Z[:, b, :]))
                        if COARSE[n]:
                            ch.link(nc.vector.memset(S(L_), float(LEAST_BITS)))
                            for it in range(COARSE[n]):
                                half = float(RANGE_BITS >> (it + 1))
                                ch.link(nc.vector.tensor_scalar(S(TB).bitcast(I32), S(L_), half, None, ALU.add))
                                for s in range(G):
                                    ch.mark(nc.vector.scalar_tensor_tensor(
                                        out=waste[:, s, :], in0=prob[:, b, s, :], scalar=S1(TB, s),
                                        in1=prob[:, b, s, :], op0=ALU.is_gt, op1=ALU.mult, accum_out=S1(F_, s)))
                                ch.sync()
                                ch.link(nc.vector.tensor_tensor(S(GE), S(F_), S(T_), ALU.is_ge))
                                ch.link(nc.vector.scalar_tensor_tensor(out=S(L_), in0=S(GE), scalar=half, in1=S(L_),
                                                                       op0=ALU.mult, op1=ALU.add))
                            ch.link(nc.vector.tensor_scalar(S(TB).bitcast(I32), S(L_),
                                                            float(RANGE_BITS >> COARSE[n]), None, ALU.add))
                            dve.wait_ge(tq_done, gg * 4 * G + 1)
                            for s in range(G):
                                ch.mark(nc.vector.scalar_tensor_tensor(
                                    out=mk[:, s, :], in0=prob[:, b, s, :], scalar=S1(TB, s), in1=prob[:, b, s, :],
                                    op0=ALU.is_le, op1=ALU.mult, accum_out=S1(Q_, s)))
                            ch.sync()
                            ch.mark(nc.vector.tensor_tensor(S(FH), Z[:, b, :], S(Q_), ALU.subtract))
                        else:
                            ch.mark(nc.vector.memset(S(FH), 0.0))
                        dve.drain()
                        for s in range(G):
                            for j in range(NSEG):
                                src = mk[:, s, j * SEG:(j + 1) * SEG] if COARSE[n] else prob[:, b, s, j * SEG:(j + 1) * SEG]
                                nc.vector.max(cand[:, s, 8 * j:8 * j + 8], src)
                        dve.drain()
                        for r in range(ROUNDS[n]):
                            for s in range(G):
                                nc.vector.max(top[:, s, 8 * r:8 * r + 8], cand[:, s, :])
                            dve.drain()
                            if r + 1 < ROUNDS[n]:
                                for s in range(G):
                                    nc.vector.match_replace(cand[:, s, :], top[:, s, 8 * r:8 * r + 8],
                                                            cand[:, s, :], -1.0)
                                dve.drain()
                        for s in range(G):
                            ch.mark(nc.vector.tensor_tensor_scan(cum[:, s, 0:R8], top[:, s, 0:R8], top[:, s, 0:R8],
                                                                 S1(FH, s), ALU.add, ALU.max))
                        ch.sync()
                        ch.link(nc.vector.tensor_tensor(cum[:, :, 0:R8], cum[:, :, 0:R8], top[:, :, 0:R8], ALU.subtract))
                        ch.link(nc.vector.tensor_tensor(cum[:, :, 0:R8], cum[:, :, 0:R8],
                                                        bcast(S(T_).unsqueeze(2), [P, G, R8]), ALU.is_lt))
                        ch.link(nc.vector.tensor_scalar(cum[:, :, 0:R8], cum[:, :, 0:R8], -4.0, 4.0, ALU.mult, ALU.add))
                        ch.link(nc.vector.tensor_tensor(cum[:, :, 0:R8], cum[:, :, 0:R8], top[:, :, 0:R8], ALU.add))
                        ch.link(nc.vector.tensor_reduce(S(V_), cum[:, :, 0:R8], AX_X, ALU.min))
                        if after is not None:
                            post(*after)
                        if prefetch:
                            row_max(gg + 1, 1)
                        dve.wait_ge(tq_done, gg * 4 * G + 1)
                        dve.wait_ge(pv_done, gg + 1)
                        if COARSE[n]:
                            cut_ties(b, linked)
                            ch.mark(nc.vector.tensor_tensor(S(BAD), S(F_), S(T_), ALU.is_ge))
                            ch.link(nc.vector.tensor_tensor(S(BAD2), S(LAST), S(T_), ALU.is_lt))
                        else:
                            for s in range(G):
                                ch.mark(nc.vector.scalar_tensor_tensor(
                                    out=mk[:, s, :], in0=prob[:, b, s, :], scalar=S1(V_, s), in1=prob[:, b, s, :],
                                    op0=ALU.is_ge, op1=ALU.mult, accum_out=S1(SM, s)))
                            ch.sync()
                            ch.mark(nc.vector.tensor_tensor(S(BAD), S(SM), S(T_), ALU.is_lt))
                            ch.link(nc.vector.tensor_tensor(S(F_), S(SM), S(V_), ALU.subtract))
                            ch.link(nc.vector.tensor_tensor(S(BAD2), S(F_), S(T_), ALU.is_ge))
                        ch.link(nc.vector.tensor_tensor(S(BAD), S(BAD), S(BAD2), ALU.max))
                        ch.link(nc.vector.tensor_tensor(flag[:, 0:1], S1(BAD, 0), S1(BAD, 1), ALU.max))
                        ch.link(nc.vector.transpose(flagT[:, :], flag[:, :]))
                        ch.link(nc.vector.tensor_reduce(any4[:, :], flagT[:, :], AX_X, ALU.max))
                        nc.vector.tensor_copy(any4i[:, :], any4[:, :])
                        dve.drain()
                        bad = [dve.value_load(any4i[q * 32:q * 32 + 1, 0:1], min_val=0, max_val=1) for q in range(4)]
                        with dve.If(bad[0] + bad[1] + bad[2] + bad[3] > 0):
                            exact(b)
                            cut_ties(b, drained)
                        ch.link(nc.vector.tensor_tensor(S(SM), S(SM), S(ZR), ALU.mult))
                        ch.link(nc.vector.tensor_scalar(S(SM), S(SM), 1e-12, None, ALU.max))
                        ch.link(nc.vector.reciprocal(S(SM), S(SM)))
                        nc.vector.tensor_tensor(fsc[:, b, :], S(SM), S(ZR), ALU.mult).then_inc(m_ready, 1)

                    row_max(base, 0)
                    row_max(base, 1)

                    def post_of(g, b):
                        return g + base, g * G, b

                    group(0, 0, True, None)
                    with dve.Fori(0, (NG - 2) // 2) as h:
                        ch.enter(h, MARKS[n])
                        for k in range(2):
                            g = h * 2 + (1 + k)
                            group(g, (1 + k) % 2, True, post_of(g - 1, k % 2))
                        ch.leave((NG - 2) // 2)
                    group(NG - 1, (NG - 1) % 2, False, post_of(NG - 2, (NG - 2) % 2))
                    post(*post_of(NG - 1, (NG - 1) % 2))
                    chain_v[0] = ch.n
                    dve.wait_ge(m_ready, base + NG + 2)

                @block.scalar
                def _(act):
                    if n == 0:
                        act.sem_inc(mt_out, 2)
                        act.sem_inc(post_a, 1)
                    for c in range(1, NC, 2):
                        act.wait_ge(c_xT_done, n * NC + c + 1)
                        nc.scalar.activation(xnT[:, c * CH:(c + 1) * CH], bank[:, 4 + c, :], ACT.Copy
                                             ).then_inc(c_xT_out, 1)
                    for c in range(1, NC, 2):
                        act.wait_ge(c_kq_done, n * NC + c + 1)
                        nc.scalar.activation(kq[:, c * CH:(c + 1) * CH], bank[:, c, :], ACT.Copy).then_inc(c_kq_out, 1)
                    act.wait_ge(c_kq_out, n * NC + NC)

                    def take_q(g, b):
                        nc.scalar.activation(qst[:, b, :], kq[DA:2 * DA, bass.ds(g * GW, GW)], ACT.Copy
                                             ).then_inc(q_ready, 1)

                    def exp(g, b, s):
                        gg = g + base
                        act.wait_ge(nm_ready, gg * G + (s + 1))
                        act.wait_ge(m_ready, gg + 1)
                        nc.scalar.activation(prob[:, b, s, :], bank[:, 0:4, :].rearrange("p b n -> p (b n)"), ACT.Exp,
                                             bias=negm[:, s:s + 1], accum_out=Z[:, b, s:s + 1]).then_inc(p_ready, 1)

                    def iteration(g, b, after, prefetch, q_next):
                        gg = g + base
                        if prefetch:
                            exp(g + 1, 1 - b, 0)
                        if q_next:
                            take_q(g + 2, b)
                        if after and not last:
                            act.wait_ge(post_v, gg + 1)
                            act.wait_ge(split_done, n + 1)
                            for s in range(G):
                                t = (g - 1) * G + s
                                nc.scalar.activation(xf2[:, bass.ds(t, 1), :].rearrange("p a d -> p (a d)"),
                                                     bank[:, 4, s * P:(s + 1) * P], ACT.Copy,
                                                     scale=rinv[:, bass.ds(t, 1)])
                                ins = nc.scalar.activation(xa2[:, bass.ds(t, 1), :].rearrange("p a d -> p (a d)"),
                                                           bank[:, 7, s * P:(s + 1) * P], ACT.Copy,
                                                           scale=fsc[:, 1 - b, s:s + 1])
                            ins.then_inc(post_a, 1)
                        if prefetch:
                            exp(g + 1, 1 - b, 1)
                        act.wait_ge(rx_done, gg + 1)
                        nc.scalar.activation(GTs[:, :], bank[:, 4, 0:GW], ACT.Copy).then_inc(gts_out, 1)
                        for s in range(G):
                            for q in range(4):
                                act.wait_ge(tq_done, gg * 4 * G + (s * 4 + q + 2))
                                nc.scalar.activation(MT[:, 4 * q:4 * q + 4, s * P:(s + 1) * P],
                                                     bank[:, 5 + q % 2, :].rearrange("p (j i) -> p j i", j=4),
                                                     ACT.Copy).then_inc(mt_out, 1)
                        act.wait_ge(pv_done, gg + 2)
                        nc.scalar.activation(ZTs[:, :], bank[:, 7, 0:GW], ACT.Copy).then_inc(zts_out, 1)

                    take_q(0, 0)
                    take_q(1, 1)
                    for s in range(G):
                        exp(0, 0, s)
                    iteration(0, 0, False, True, True)
                    with act.Fori(0, (NG - 4) // 2) as h:
                        for k in range(2):
                            g = h * 2 + (1 + k)
                            iteration(g, (1 + k) % 2, True, True, True)
                    for g in range(NG - 3, NG):
                        iteration(g, g % 2, True, g + 1 < NG, g + 2 < NG)
                    if not last:
                        b = (NG - 1) % 2
                        act.wait_ge(post_v, base + NG + 1)
                        for s in range(G):
                            t = (NG - 1) * G + s
                            nc.scalar.activation(xf2[:, t, :], bank[:, 4, s * P:(s + 1) * P], ACT.Copy,
                                                 scale=rinv[:, t:t + 1])
                            ins = nc.scalar.activation(xa2[:, t, :], bank[:, 7, s * P:(s + 1) * P], ACT.Copy,
                                                       scale=fsc[:, b, s:s + 1])
                        ins.then_inc(post_a, 1)

                @block.tensor
                def _(pe):
                    if n == 0:
                        pe.sem_inc(tq_done, 1)
                        pe.sem_inc(pv_done, 1)
                        pe.sem_inc(c_xn, 1)
                    transpose_in(pe, xsrc[:, :, :], c_xn, 1, c_xT_done)
                    pe.wait_ge(c_xT_out, n * NC + NC)
                    for c in range(NC):
                        nc.tensor.matmul(bank[:, c, :], wkq[:, :], xnT[:, c * CH:(c + 1) * CH], start=True, stop=True
                                         ).then_inc(c_kq_done, 1)
                    pe.wait_ge(c_kq_out, n * NC + NC)

                    def logits(g, b, s):
                        gg = g + base
                        pe.wait_ge(q_ready, gg + 1)
                        if s or not (isinstance(g, int) and g == 0):
                            pe.wait_ge(p_ready, gg * G + s)
                        for c in range(NC):
                            mm = nc.tensor.matmul(bank[:, c, :], qst[:, b, s * P:(s + 1) * P],
                                                  kq[0:DA, c * CH:(c + 1) * CH], start=True, stop=True)
                        mm.then_inc(l_done, 1)

                    def iteration(g, b, l1, l2):
                        gg = g + base
                        if l1:
                            logits(g + 1, 1 - b, 1)
                        pe.wait_ge(split_done, n + 1)
                        pe.wait_ge(post_v if last else post_a, gg + 1)
                        for jt in range(NT):
                            for k in range(3):
                                mm = nc.tensor.matmul(bank[:, 4, 0:GW], parts[:, k, jt, :],
                                                      adjT[:, jt, bass.ds(g * GW, GW)],
                                                      start=(jt == 0 and k == 0), stop=(jt == NT - 1 and k == 2))
                        mm.then_inc(rx_done, 1)
                        if l2:
                            logits(g + 2, b, 0)
                        pe.wait_ge(m_ready, gg + 3)
                        for s in range(G):
                            for q in range(4):
                                pe.wait_ge(mt_out, gg * 4 * G + (s * 4 + q + 1))
                                for j in range(4):
                                    jt = 4 * q + j
                                    mm = nc.tensor.transpose(bank[:, 5 + q % 2, j * P:(j + 1) * P],
                                                             mk[:, s, jt * P:(jt + 1) * P], ident[:, :])
                                mm.then_inc(tq_done, 1)
                        pe.wait_ge(mt_out, gg * 4 * G + (4 * G + 2))
                        for jt in range(NT):
                            mm = nc.tensor.matmul(bank[:, 7, 0:GW], xsrc[:, jt, :], MT[:, jt, :], start=(jt == 0),
                                                  stop=(jt == NT - 1))
                        mm.then_inc(pv_done, 1)
                        pe.wait_ge(gts_out, gg + 1)
                        pe.wait_ge(zts_out, gg + 1)
                        for s in range(G):
                            for src, bk, u in ((GTs, 4, 2 * n), (ZTs, 7, 2 * n + 1)):
                                sl = src[:, s * P:(s + 1) * P]
                                mm = nc.tensor.matmul(bank[:, bk, GW + s * P:GW + (s + 1) * P], sl, UT[:, u, :],
                                                      start=True, stop=True)
                                if not last:
                                    mm = nc.tensor.transpose(bank[:, bk, s * P:(s + 1) * P], sl, ident[:, :])
                        mm.then_inc(post_done, 1)

                    logits(0, 0, 0)
                    logits(0, 0, 1)
                    logits(1, 1, 0)
                    iteration(0, 0, True, True)
                    with pe.Fori(0, (NG - 4) // 2) as h:
                        for k in range(2):
                            iteration(h * 2 + (1 + k), (1 + k) % 2, True, True)
                    for g in range(NG - 3, NG):
                        iteration(g, g % 2, g + 1 < NG, g + 2 < NG)

        for n in range(STEPS):
            step_block(n)

        lng, lnb, lnu = carve(D, D, NT * D)
        lnu = lnu.rearrange("p (t d) -> p t d", t=NT)
        with nc.Block() as block:
            @block.sync
            def _(sp):
                sp.dma_start(lng, bcast(L1_gnn_ln_g.rearrange("(a n) -> a n", a=1), [P, D])).then_inc(c_ld, 16)
                sp.dma_start(lnb, bcast(L1_gnn_ln_b.rearrange("(a n) -> a n", a=1), [P, D])).then_inc(c_ld, 16)

            @block.gpsimd
            def _(pool):
                pool_pow(pool, 4)

            @block.vector
            def _(dve):
                ch = Chain(dve, cch_v)
                ch.n = chain_v[0]
                moments(dve, ch, hacc)
                normalise(dve, ch, lnu, hacc[:, :, :], 0)
                dve.wait_ge(c_ld, 16 * (5 + 2 * STEPS))
                b3 = [P, NT, D]
                ch.link(nc.vector.tensor_tensor(lnu, lnu, bcast(lng.unsqueeze(1), b3), ALU.mult))
                ch.link(nc.vector.tensor_tensor(lnu, lnu, bcast(lnb.unsqueeze(1), b3), ALU.add))
                ch.link(nc.vector.tensor_tensor(res[:, :, :], res[:, :, :], lnu, ALU.add))
                chain_v[0] = ch.n

        if stop_after == "C":
            with nc.Block() as block:
                @block.sync
                def _(sp):
                    sp.dma_start(out.rearrange("(t p) d -> p t d", p=P), res[:, :, :]).then_inc(finish_early, 16)
                    sp.wait_ge(finish_early, 16)
            return

        ED, HD = L1_ffn_W1.shape[0], L1_ffn_W1.shape[2]
        HCD = HD // P
        CAPACITY = float(math.ceil(N * 1.25 / ED))
        (dw1, dw2, dw2s, db1, db2, hid, y, gam, bet, meanb, wr, brb, rs8) = carve(
            2 * HD, 2 * HCD * D, 2 * HCD * D, 2 * HCD, 2 * D, 2 * HCD * N // 2, NT * D, D, D, P, ED, ED, 80)
        dw1 = dw1.rearrange("p (k h) -> p k h", k=2)
        dw2, dw2s = (v.rearrange("p (k c d) -> p k c d", k=2, c=HCD) for v in (dw2, dw2s))
        db1 = db1.rearrange("p (k c) -> p k c", k=2)
        db2 = db2.rearrange("p (k d) -> p k d", k=2)
        hid = hid.rearrange("p (b u n) -> p b u n", b=2, u=2 * HCD)
        y = y.rearrange("p (t d) -> p t d", t=NT)
        r8 = rs8.rearrange("p (k e) -> p k e", k=10)
        (LG, MX, EX, RW, LD, M8, SC) = range(7)
        idx8 = sb("idx8", [P, 8], U32)
        one = [r8[:, 7 + k // 8, k % 8:k % 8 + 1] for k in range(24)]

        (d_ldr, d_ldg, d_xn, d_mean_done, d_meanb_out, d_lg_done, d_nm, d_ex, d_nm2, d_ex2, d_top, d_e21, d_idx) = names(
            "d", "ldr", "ldg", "xn", "mean_done", "meanb_out", "lg_done", "nm", "ex", "nm2", "ex2", "top", "e21",
            "idx")
        (d_w1, d_w2, d_w2s, d_xT_done, d_xT_out, d_h_done, d_hid, d_y_done, d_store, d_out, dch_v, d_y_out) = names(
            "d", "w1_ld", "w2_ld", "w2_scaled", "xT_done", "xT_out", "h_done", "hid", "y_done", "store", "out", "ch_v",
            "y_out")

        with nc.Block() as block:
            @block.sync
            def _(sp):
                def row(v, width):
                    return bcast(v.rearrange("(a n) -> a n", a=1), [P, width])

                sp.dma_start(wr, L1_ffn_Wr).then_inc(d_ldr, 16)
                sp.dma_start(brb, row(L1_ffn_br, ED)).then_inc(d_ldr, 16)
                sp.dma_start(gam, row(L1_ffn_gamma, D)).then_inc(d_ldg, 16)
                sp.dma_start(bet, row(L1_ffn_beta, D)).then_inc(d_ldg, 16)
                sp.wait_ge(d_idx, 1)
                for k in range(2):
                    e = bass.ds(sp.value_load(idx8[0:1, k:k + 1], min_val=0, max_val=ED - 1), 1)
                    sp.dma_start(dw1[:, k, :], L1_ffn_W1[e].rearrange("a p h -> (a p) h")).then_inc(d_w1, 16)
                    with nc.allow_non_contiguous_dma("a bias of one float per partition"):
                        sp.dma_start(db1[:, k, :], L1_ffn_b1[e, :].rearrange("a (c p) -> (a p) c", p=P)
                                     ).then_inc(d_w1, 16)
                    sp.dma_start(dw2[:, k, :, :], L1_ffn_W2[e].rearrange("a (c p) d -> (a p) c d", p=P)
                                 ).then_inc(d_w2, 16)
                    sp.dma_start(db2[:, k, :], bcast(L1_ffn_b2[e, :], [P, D])).then_inc(d_w2, 16)
                for c in range(NC):
                    sp.wait_ge(d_out, c + 1)
                    sp.dma_start(out.rearrange("(t p) d -> p t d", p=P)[:, c * TPC:(c + 1) * TPC, :],
                                 res[:, c * TPC:(c + 1) * TPC, :]).then_inc(d_store, 16)
                sp.wait_ge(d_store, 16 * NC)

            @block.gpsimd
            def _(pool):
                pool_pow(pool, 5)
                pool_pow(pool, 6)

            @block.vector
            def _(dve):
                ch = Chain(dve, dch_v)
                moments(dve, ch, res)
                normalise(dve, ch, xn[:, :, :], res[:, :, :], 0)
                dve.sem_inc(d_xn, 1)
                dve.wait_ge(d_mean_done, 1)
                nc.vector.tensor_scalar(meanb, ones[:, :], bank[:, 0, 0:1], 1.0 / N, ALU.mult, ALU.mult
                                        ).then_inc(d_meanb_out, 1)
                for c in range(0, NC, 2):
                    dve.wait_ge(d_xT_done, c + 1)
                    nc.vector.tensor_copy(xnT[:, c * CH:(c + 1) * CH], bank[:, 4 + c, :]).then_inc(d_xT_out, 1)
                dve.wait_ge(d_ldr, 32)
                dve.wait_ge(d_lg_done, 1)
                ch.link(nc.vector.tensor_tensor(r8[:, LG, :], bank[:, 0, 8:8 + ED], brb, ALU.add))
                ch.link(nc.vector.max(r8[:, MX, :], r8[:, LG, :]))
                nc.vector.tensor_scalar(one[0], r8[:, MX, 0:1], -1.0, None, ALU.mult).then_inc(d_nm, 1)
                dve.wait_ge(d_ex, 1)
                ch.link(nc.vector.reciprocal(one[2], one[1]))
                ch.link(nc.vector.tensor_scalar(r8[:, RW, :], r8[:, EX, :], one[2], None, ALU.mult))
                ch.link(nc.vector.tensor_scalar(r8[:, LD, :], r8[:, RW, :], float(N), CAPACITY, ALU.mult, ALU.max))
                ch.link(nc.vector.reciprocal(r8[:, SC, :], r8[:, LD, :]))
                ch.link(nc.vector.tensor_scalar(r8[:, SC, :], r8[:, SC, :], CAPACITY, 1.0, ALU.mult, ALU.min))
                ch.link(nc.vector.tensor_tensor(r8[:, RW, :], r8[:, RW, :], r8[:, SC, :], ALU.mult))
                ch.link(nc.vector.max(r8[:, MX, :], r8[:, RW, :]))
                nc.vector.tensor_scalar(one[3], r8[:, MX, 0:1], -1.0, None, ALU.mult).then_inc(d_nm2, 1)
                dve.wait_ge(d_ex2, 1)
                ch.link(nc.vector.reciprocal(one[5], one[4]))
                ch.link(nc.vector.tensor_scalar(r8[:, EX, :], r8[:, EX, :], one[5], None, ALU.mult))
                ch.link(nc.vector.max(r8[:, M8, :], r8[:, EX, :]))
                nc.vector.max_index(idx8[:, :], r8[:, M8, :], r8[:, EX, :]).then_inc(d_idx, 1)
                nc.vector.tensor_tensor(one[6], r8[:, M8, 1:2], r8[:, M8, 0:1], ALU.subtract).then_inc(d_top, 1)
                dve.wait_ge(d_e21, 1)
                ch.link(nc.vector.tensor_scalar(one[8], one[7], 1.0, None, ALU.add))
                ch.link(nc.vector.reciprocal(one[8], one[8]))
                ch.link(nc.vector.tensor_tensor(one[9], one[7], one[8], ALU.mult))
                dve.wait_ge(d_w2, 64)
                for k in range(2):
                    nc.vector.tensor_scalar(dw2s[:, k, :, :], dw2[:, k, :, :], one[8 + k], None, ALU.mult
                                            ).then_inc(d_w2s, 1)
                ch.link(nc.vector.tensor_scalar(db2[:, 0, :], db2[:, 0, :], one[8], None, ALU.mult))
                ch.link(nc.vector.scalar_tensor_tensor(out=db2[:, 0, :], in0=db2[:, 1, :], scalar=one[9],
                                                       in1=db2[:, 0, :], op0=ALU.mult, op1=ALU.add))
                ch.link(nc.vector.tensor_tensor(xn[:, :, :], xn[:, :, :],
                                                bcast(db2[:, 0, :].unsqueeze(1), [P, NT, D]), ALU.add))
                for c in range(NC):
                    dve.wait_ge(d_y_done, c + 1)
                    ts = slice(c * TPC, (c + 1) * TPC)
                    ch.mark(nc.vector.tensor_tensor(y[:, ts, :], bank[:, 4 + c, :].rearrange("p (t d) -> p t d", t=TPC),
                                                    xn[:, ts, :], ALU.add))
                ch.sync()
                moments(dve, ch, y)
                dve.wait_ge(d_ldg, 32)
                normalise(dve, ch, y, y, 0)
                b3 = [P, TPC, D]
                for c in range(NC):
                    ts = slice(c * TPC, (c + 1) * TPC)
                    ch.link(nc.vector.tensor_tensor(y[:, ts, :], y[:, ts, :], bcast(gam.unsqueeze(1), b3), ALU.mult))
                    ch.link(nc.vector.tensor_tensor(y[:, ts, :], y[:, ts, :], bcast(bet.unsqueeze(1), b3), ALU.add))
                    nc.vector.tensor_tensor(res[:, ts, :], res[:, ts, :], y[:, ts, :], ALU.add).then_inc(d_out, 1)
                dve.wait_ge(d_out, NC)

            @block.scalar
            def _(act):
                for c in range(1, NC, 2):
                    act.wait_ge(d_xT_done, c + 1)
                    nc.scalar.activation(xnT[:, c * CH:(c + 1) * CH], bank[:, 4 + c, :], ACT.Copy).then_inc(d_xT_out, 1)
                act.wait_ge(d_nm, 1)
                nc.scalar.activation(r8[:, EX, :], r8[:, LG, :], ACT.Exp, bias=one[0], accum_out=one[1]).then_inc(d_ex, 1)
                act.wait_ge(d_nm2, 1)
                nc.scalar.activation(r8[:, EX, :], r8[:, RW, :], ACT.Exp, bias=one[3], accum_out=one[4]).then_inc(d_ex2, 1)
                act.wait_ge(d_top, 1)
                nc.scalar.activation(one[7], one[6], ACT.Exp).then_inc(d_e21, 1)
                act.wait_ge(d_w1, 64)
                for c in range(NC):
                    for u in range(2 * HCD):
                        v = c * 2 * HCD + u
                        act.wait_ge(d_h_done, v + 1)
                        if u == 0 and c >= 2:
                            act.wait_ge(d_y_done, c - 1)
                        nc.scalar.activation(hid[:, c % 2, u, :], bank[:, v % 4, :], ACT.Gelu,
                                             bias=db1[:, u // HCD, u % HCD:u % HCD + 1]).then_inc(d_hid, 1)

            @block.tensor
            def _(pe):
                pe.wait_ge(d_xn, 1)
                for t in range(NT):
                    mm = nc.tensor.matmul(bank[:, 0, 0:1], xn[:, t, :], ones[:, 0:1], start=(t == 0), stop=(t == NT - 1))
                mm.then_inc(d_mean_done, 1)
                pe.wait_ge(d_ldr, 32)
                pe.wait_ge(d_meanb_out, 1)
                nc.tensor.matmul(bank[:, 0, 8:8 + ED], meanb, wr, start=True, stop=True).then_inc(d_lg_done, 1)
                transpose_in(pe, xn[:, :, :], d_xn, 1, d_xT_done)

                def up(c):
                    for u in range(2 * HCD):
                        v = c * 2 * HCD + u
                        if v >= 4:
                            pe.wait_ge(d_hid, v - 3)
                        nc.tensor.matmul(bank[:, v % 4, :], dw1[:, u // HCD, (u % HCD) * P:(u % HCD + 1) * P],
                                         xnT[:, c * CH:(c + 1) * CH], start=True, stop=True).then_inc(d_h_done, 1)

                pe.wait_ge(d_w1, 64)
                pe.wait_ge(d_xT_out, NC)
                pe.wait_ge(d_nm, 1)
                up(0)
                pe.wait_ge(d_w2s, 2)
                for c in range(NC):
                    if c + 1 < NC:
                        up(c + 1)
                    pe.wait_ge(d_hid, (c + 1) * 2 * HCD)
                    for t in range(TPC):
                        for u in range(2 * HCD):
                            mm = nc.tensor.matmul(bank[:, 4 + c, t * P:(t + 1) * P], hid[:, c % 2, u, t * P:(t + 1) * P],
                                                  dw2s[:, u // HCD, u % HCD, :], start=(u == 0), stop=(u == 2 * HCD - 1))
                    mm.then_inc(d_y_done, 1)


_INS = ("x", "adj", "L0_gnn_W", "L0_gnn_bias", "L0_gnn_b", "L0_ffn_gate_w", "L0_ffn_gate_b", "L0_ffn_w1", "L0_ffn_w2",
        "L0_ffn_w3", "L1_gnn_W1", "L1_gnn_W2", "L1_gnn_W3", "L1_gnn_U1", "L1_gnn_U2", "L1_gnn_ln_g", "L1_gnn_ln_b",
        "L1_ffn_Wr", "L1_ffn_br", "L1_ffn_W1", "L1_ffn_b1", "L1_ffn_W2", "L1_ffn_b2", "L1_ffn_gamma", "L1_ffn_beta")


def kernel(**inputs):
    import concourse.bacc as bacc
    import numpy as np
    from concourse.bass_utils import run_bass_kernel_spmd

    nc = bacc.Bacc("TRN2", target_bir_lowering=False, num_devices=1)
    arrays, args = {}, []
    for name in _INS:
        a = np.ascontiguousarray(inputs[name])
        arrays[f"in_{name}_dram"] = a
        args.append(nc.dram_tensor(f"in_{name}_dram", a.shape, mybir.dt.from_np(a.dtype), kind="ExternalInput").ap())
    out = nc.dram_tensor("out_dram", (N, D), F32, kind="ExternalOutput").ap()
    build(nc, *args, out)
    r = run_bass_kernel_spmd(nc, [arrays], core_ids=[0])
    return r.results[0]["out_dram"]
```
